# Optimizing a Trainium2 kernel written in Bass

```python
import numpy as np
import jax
import jax.numpy as jnp

def _softmax(x, axis=-1):
    return jax.nn.softmax(x, axis=axis)

def _gelu(x):
    return jax.nn.gelu(x, approximate=True)

def _silu(x):
    return jax.nn.silu(x)

def _sigmoid(x):
    return jax.nn.sigmoid(x)

def _layernorm(x, axis=-1, eps=1e-05):
    m = jnp.mean(x, axis=axis, keepdims=True)
    v = jnp.var(x, axis=axis, keepdims=True)
    return (x - m) / jnp.sqrt(v + eps)

def _scatter_add(tgt, idx, src, axis=0):
    return tgt.at[idx].add(src)

def _segment_sum(src, seg, n):
    return jax.ops.segment_sum(src, seg, n)
kernel_name = 'mk_rec_standalone_d1_rec_r8_06926e'

def setup_inputs(seed: int=0):
    np.random.seed(seed)
    _w = jnp.asarray

    def _rec_inputs():
        import jax
        import jax.numpy as jnp
        _rk = jax.random.key(seed)
        r_inputs = -0.000292821 + 1.00034 * jax.random.normal(jax.random.fold_in(_rk, 1), (1024, 32, 64), jnp.float32)
        return r_inputs
    r_inputs = _rec_inputs()

    def _L0_rec_setup():
        import jax, jax.numpy as jnp
        import numpy as np
        B, F_SIZE, DIM = (256, 32, 64)
        LAYER_SIZES = (128, 128)

        def _cin_forward(inputs, Ws, bs):
            batch, _, dim = inputs.shape
            x0 = inputs
            h = inputs
            finals = []
            n_layers = len(Ws)
            for i in range(n_layers):
                H = h.shape[1]
                M = x0.shape[1]
                z = jnp.einsum('bhd,bmd->bhmd', h, x0).reshape(batch, H * M, dim)
                out = jnp.einsum('bcd,oc->bod', z, Ws[i]) + bs[i][None, :, None]
                out = jax.nn.relu(out)
                size = Ws[i].shape[0]
                if i != n_layers - 1:
                    h = out[:, :size // 2, :]
                    finals.append(out[:, size // 2:, :])
                else:
                    finals.append(out)
            result = jnp.concatenate(finals, axis=1)
            return jnp.sum(result, axis=-1)
        key = jax.random.key(seed)
        k1, k2, k3 = jax.random.split(key, 3)
        inputs = jax.random.normal(k1, (B, F_SIZE, DIM), dtype=jnp.float32)
        W0 = jax.random.normal(k2, (128, F_SIZE * F_SIZE), dtype=jnp.float32) * 0.03
        b0 = jnp.zeros((128,), dtype=jnp.float32)
        W1 = jax.random.normal(k3, (128, 64 * F_SIZE), dtype=jnp.float32) * 0.03
        b1 = jnp.zeros((128,), dtype=jnp.float32)
        return {'inputs': inputs, 'W0': W0, 'b0': b0, 'W1': W1, 'b1': b1}
    _L0_rec_all = _L0_rec_setup()
    _L0_rec_in = {k: v for k, v in _L0_rec_all.items() if k in ('W0', 'b0', 'W1', 'b1')}
    del _L0_rec_all
    return {'r_inputs': r_inputs, 'L0_rec_W0': _L0_rec_in['W0'], 'L0_rec_b0': _L0_rec_in['b0'], 'L0_rec_W1': _L0_rec_in['W1'], 'L0_rec_b1': _L0_rec_in['b1']}

def reference(r_inputs, L0_rec_W0, L0_rec_b0, L0_rec_W1, L0_rec_b1):
    import jax
    import jax.numpy as jnp

    def _L0_rec_ref(inputs, W0, b0, W1, b1):
        import jax, jax.numpy as jnp
        import numpy as np
        B, F_SIZE, DIM = (256, 32, 64)
        LAYER_SIZES = (128, 128)

        def _cin_forward(inputs, Ws, bs):
            batch, _, dim = inputs.shape
            x0 = inputs
            h = inputs
            finals = []
            n_layers = len(Ws)
            for i in range(n_layers):
                H = h.shape[1]
                M = x0.shape[1]
                z = jnp.einsum('bhd,bmd->bhmd', h, x0).reshape(batch, H * M, dim)
                out = jnp.einsum('bcd,oc->bod', z, Ws[i]) + bs[i][None, :, None]
                out = jax.nn.relu(out)
                size = Ws[i].shape[0]
                if i != n_layers - 1:
                    h = out[:, :size // 2, :]
                    finals.append(out[:, size // 2:, :])
                else:
                    finals.append(out)
            result = jnp.concatenate(finals, axis=1)
            return jnp.sum(result, axis=-1)
        return _cin_forward(inputs, (W0, W1), (b0, b1))
    y = _L0_rec_ref(r_inputs, L0_rec_W0, L0_rec_b0, L0_rec_W1, L0_rec_b1)
    return y

_drawn_inputs = setup_inputs


def setup_inputs(seed=0):
    import zlib

    import numpy as np

    out = dict(_drawn_inputs(seed))
    spreads = {'L0_rec_b0': (0.0, 0.1), 'L0_rec_b1': (0.0, 0.1)}
    factors = {}
    for name, (base, spread) in spreads.items():
        noise = np.random.default_rng([zlib.crc32(name.encode()), seed]).standard_normal(out[name].shape)
        drawn = base * np.exp(spread * noise) if base else spread * noise
        out[name] = jnp.asarray(drawn.astype(out[name].dtype))
    for name, factor in factors.items():
        out[name] = (out[name] * factor).astype(out[name].dtype)
    return out
```

```python
from contextlib import ExitStack

import concourse.bass as bass
from concourse import mybir

F32 = mybir.dt.float32
F32R = mybir.dt.float32r
ALU = mybir.AluOpType
ACT = mybir.ActivationFunctionType
AX_X = mybir.AxisListType.X

P = 128
N = 512
DIM = 64
BPC = N // DIM
BODY = 4
RING = 4
GPC = 5
LOADS = 5


def past(count, n):
    return not isinstance(count, int) or count >= n


def build(nc, xT, w0, w0swap, w1, wuv, sel, b0, b1, outT):
    S = xT.shape[1]
    CHUNKS = S // N
    BATCH = S // DIM
    assert CHUNKS % BODY == 0 and (BODY * GPC) % RING == 0

    with ExitStack() as ctx:
        def sb(name, shape, dt=F32):
            return ctx.enter_context(nc.sbuf_tensor(name, shape, dt))

        def sem(name):
            return ctx.enter_context(nc.semaphore(name))

        q = sb("q", [P, BODY, 4, N])
        a = sb("a", [P, BODY, N])
        uv = sb("uv", [P, BODY, 2, N])
        z = sb("z", [P, RING, 4, N])
        zuv = sb("zuv", [P, 2, N])
        w0_sb = sb("w0_sb", [P, 4, P])
        w0s_sb = sb("w0s_sb", [P, 4, P])
        w1_sb = sb("w1_sb", [P, 16, P])
        wuv_sb = sb("wuv_sb", [P, P])
        sel_sb = sb("sel_sb", [P, 4, P])
        selr = sb("selr", [P, 4, P], F32R)
        b0_sb = sb("b0_sb", [P, 1])
        b1_sb = sb("b1_sb", [P, 1])
        r0 = sb("r0", [P, 2, N])
        hs = sb("hs", [P, 2, N], F32R)
        r1 = sb("r1", [P, 2, N])
        sum0 = sb("sum0", [P, BATCH])
        sum1 = sb("sum1", [P, BATCH])

        p_ps = ctx.enter_context(nc.psum_tensor("p_ps", [P, 4, N], F32))
        out0 = ctx.enter_context(nc.psum_tensor("out0", [P, 2, N], F32))
        out1 = ctx.enter_context(nc.psum_tensor("out1", [P, 2, N], F32))

        weights_loaded = sem("weights_loaded")
        x_loaded = [sem(f"x_loaded{s}") for s in range(BODY)]
        w_ready = sem("w_ready")
        sel_ready = sem("sel_ready")
        z_ready = sem("z_ready")
        zuv_ready = sem("zuv_ready")
        group_done = sem("group_done")
        layer0_done = sem("layer0_done")
        r0_ready = sem("r0_ready")
        hh_ready = sem("hh_ready")
        hl_ready = sem("hl_ready")
        p_ready = sem("p_ready")
        r1_ready = sem("r1_ready")
        sum0_ready = sem("sum0_ready")
        sum1_ready = sem("sum1_ready")
        stored = sem("stored")

        block = ctx.enter_context(nc.Block())

        def x_rows(pattern, row, c):
            return bass.AP(xT.tensor, row * S + c * N, [[st * S, n] for st, n in pattern] + [[1, N]])

        def run(eng, chunk):
            for c in range(BODY):
                chunk(c, c)
            with eng.Fori(BODY, CHUNKS - BODY, BODY) as base:
                for k in range(BODY):
                    chunk(base + k, k)
            for k in range(BODY):
                chunk(CHUNKS - BODY + k, k)

        def group1(c, j):
            return c * GPC + 2 + j - (isinstance(c, int) and c == CHUNKS - 1)

        def slot1(c, k, j):
            return (k * GPC + 2 + j - (isinstance(c, int) and c == CHUNKS - 1)) % RING

        def visit(c):
            return c // BODY + 1

        @block.sync
        def _(sp):
            def load(c, k):
                if past(c, BODY):
                    sp.wait_ge(z_ready, (c - BODY) * GPC + 6)
                sp.dma_start(q[:, k], x_rows([(0, 16), (4, 8), (1, 4)], 0, c)).then_inc(x_loaded[k], 16)
                sp.dma_start(a[0:96, k], x_rows([(4, 3), (1, 4), (4, 8)], 4, c)).then_inc(x_loaded[k], 16)
                sp.dma_start(a[96:128, k], x_rows([(1, 4), (4, 8)], 44, c)).then_inc(x_loaded[k], 16)
                sp.dma_start(uv[:, k, 0], x_rows([(0, 8), (1, 16)], 0, c)).then_inc(x_loaded[k], 16)
                sp.dma_start(uv[:, k, 1], x_rows([(0, 2), (1, 64)], 76, c)).then_inc(x_loaded[k], 16)

            run(sp, load)
            sp.wait_ge(sum0_ready, CHUNKS)
            sp.wait_ge(sum1_ready, CHUNKS)
            sp.dma_start(outT[0:64, :], sum0[64:128, :]).then_inc(stored, 16)
            sp.dma_start(outT[64:192, :], sum1[:, :]).then_inc(stored, 16)
            sp.wait_ge(stored, 32)

        @block.scalar
        def _(act):
            for dst, src in ((w0_sb, w0), (w0s_sb, w0swap), (w1_sb, w1), (wuv_sb, wuv), (sel_sb, sel), (b0_sb, b0), (b1_sb, b1)):
                act.dma_start(dst[:], src).then_inc(weights_loaded, 16)
            act.wait_ge(weights_loaded, 7 * 16)
            nc.scalar.activation(selr[:], sel_sb[:], ACT.Copy).then_inc(sel_ready, 1)

            def relu0(c, k):
                act.wait_ge(layer0_done, c + 1)
                if past(c, 2):
                    act.wait_ge(sum0_ready, c - 1)
                    act.wait_ge(hl_ready, c - 1)
                    act.wait_ge(p_ready, c - 1)
                nc.scalar.activation(r0[:, k % 2], out0[:, k % 2], ACT.Relu, bias=b0_sb[:]).then_inc(r0_ready, 1)
                nc.scalar.activation(hs[0:64, k % 2], out0[0:64, k % 2], ACT.Relu, bias=b0_sb[0:64]).then_inc(hh_ready, 1)

            def relu1(c, k):
                act.wait_ge(group_done, group1(c, 3) + 1)
                if past(c, 2):
                    act.wait_ge(sum1_ready, c - 1)
                nc.scalar.activation(r1[:, k % 2], out1[:, k % 2], ACT.Relu, bias=b1_sb[:]).then_inc(r1_ready, 1)

            relu0(0, 0)

            def chunk(c, k):
                if past(c, 1):
                    relu1(c - 1, (k - 1) % BODY)
                if not (isinstance(c, int) and c + 1 >= CHUNKS):
                    relu0(c + 1, (k + 1) % BODY)

            run(act, chunk)
            relu1(CHUNKS - 1, BODY - 1)

        @block.vector
        def _(dve):
            dve.wait_ge(weights_loaded, 7 * 16)
            nc.vector.tensor_tensor(w0_sb[:], w0_sb[:], w0s_sb[:], ALU.add).then_inc(w_ready, 1)

            def products0(c, k, g, slot):
                dve.wait_ge(x_loaded[k], 16 * LOADS * visit(c))
                if past(g, RING):
                    dve.wait_ge(group_done, g - RING + 1)
                nc.vector.tensor_tensor(z[:, slot], a[:, k].unsqueeze(1).to_broadcast([P, 4, N]), q[:, k], ALU.mult).then_inc(z_ready, 1)
                if past(c, 2):
                    dve.wait_ge(layer0_done, c - 1)
                nc.vector.tensor_tensor(zuv[:, k % 2], uv[:, k, 0], uv[:, k, 1], ALU.mult).then_inc(zuv_ready, 1)

            def products1(c, k, j, g, slot):
                if j == 0:
                    dve.wait_ge(p_ready, c + 1)
                if past(g, RING):
                    dve.wait_ge(group_done, g - RING + 1)
                nc.vector.tensor_tensor(z[:, slot], p_ps[:], q[:, k, j].unsqueeze(1).to_broadcast([P, 4, N]), ALU.mult).then_inc(z_ready, 1)

            def low_h(c, k):
                dve.wait_ge(r0_ready, c + 1)
                dve.wait_ge(hh_ready, c + 1)
                nc.vector.tensor_tensor(hs[64:128, k % 2], r0[0:64, k % 2], hs[0:64, k % 2].bitcast(F32), ALU.subtract).then_inc(hl_ready, 1)

            def sums0(c, k):
                nc.vector.tensor_reduce(sum0[64:128, bass.ds(c * BPC, BPC)], r0[64:128, k % 2].rearrange("p (b d) -> p b d", d=DIM), AX_X, ALU.add).then_inc(sum0_ready, 1)

            def sums1(c, k):
                dve.wait_ge(r1_ready, c + 1)
                nc.vector.tensor_reduce(sum1[:, bass.ds(c * BPC, BPC)], r1[:, k % 2].rearrange("p (b d) -> p b d", d=DIM), AX_X, ALU.add).then_inc(sum1_ready, 1)

            products0(0, 0, 0, 0)
            products0(1, 1, 1, 1)
            low_h(0, 0)
            sums0(0, 0)

            def chunk(c, k):
                for j in range(4):
                    products1(c, k, j, group1(c, j), slot1(c, k, j))
                    if j == 2 and not (isinstance(c, int) and c + 1 >= CHUNKS):
                        low_h(c + 1, (k + 1) % BODY)
                if not (isinstance(c, int) and c + 1 >= CHUNKS):
                    sums0(c + 1, (k + 1) % BODY)
                if past(c, 1):
                    sums1(c - 1, (k - 1) % BODY)
                if not (isinstance(c, int) and c + 2 >= CHUNKS):
                    products0(c + 2, (k + 2) % BODY, c * GPC + 6, (k * GPC + 6) % RING)

            run(dve, chunk)
            sums1(CHUNKS - 1, BODY - 1)

        @block.tensor
        def _(pe):
            pe.wait_ge(w_ready, 1)
            pe.wait_ge(sel_ready, 1)

            def contract0(c, k, g, slot):
                if past(c, 2):
                    pe.wait_ge(r0_ready, c - 1)
                    pe.wait_ge(hh_ready, c - 1)
                pe.wait_ge(z_ready, g + 1)
                for j in range(4):
                    last = nc.tensor.matmul(out0[:, k % 2], w0_sb[:, j], z[:, slot, j], start=j == 0, stop=False)
                last.then_inc(group_done, 1)
                pe.wait_ge(zuv_ready, c + 1)
                nc.tensor.matmul(out0[:, k % 2], wuv_sb[0:64], zuv[0:64, k % 2], start=False, stop=True).then_inc(layer0_done, 1)

            def contract1(c, k, j, g, slot):
                if j == 0 and past(c, 2):
                    pe.wait_ge(r1_ready, c - 1)
                pe.wait_ge(z_ready, g + 1)
                for i in range(4):
                    last = nc.tensor.matmul(out1[:, k % 2], w1_sb[:, 4 * j + i], z[:, slot, i], start=j + i == 0, stop=j + i == 6)
                last.then_inc(group_done, 1)

            def select(c, k):
                pe.wait_ge(hl_ready, c + 1)
                pe.wait_ge(hh_ready, c + 1)
                if past(c, 1):
                    pe.wait_ge(z_ready, c * GPC + 1)
                for i in range(4):
                    last = nc.tensor.matmul(p_ps[:, i], selr[:, i], hs[:, k % 2], start=True, stop=True)
                last.then_inc(p_ready, 1)

            contract0(0, 0, 0, 0)
            contract0(1, 1, 1, 1)
            select(0, 0)

            def chunk(c, k):
                for j in range(4):
                    contract1(c, k, j, group1(c, j), slot1(c, k, j))
                    if j == 1 and not (isinstance(c, int) and c + 1 >= CHUNKS):
                        select(c + 1, (k + 1) % BODY)
                if not (isinstance(c, int) and c + 2 >= CHUNKS):
                    contract0(c + 2, (k + 2) % BODY, c * GPC + 6, (k * GPC + 6) % RING)

            run(pe, chunk)


def kernel(r_inputs, L0_rec_W0, L0_rec_b0, L0_rec_W1, L0_rec_b1):
    import numpy as np
    import concourse.bacc as bacc
    from concourse.bass_utils import run_bass_kernel_spmd

    x = np.asarray(r_inputs)
    B, M, D = x.shape
    xT = np.ascontiguousarray(np.transpose(x, (1, 0, 2))).reshape(M, B * D)
    f = np.arange(16)
    xT = np.concatenate([xT, xT[0:12], xT[16:32], xT[16:32]] + [xT[4 * (f // 4) + e] for e in range(4)], axis=0)

    s, i, mb = (t.reshape(-1) for t in np.meshgrid(np.arange(4), np.arange(4), np.arange(8), indexing="ij"))
    block = np.where(s < 3, (mb + s + 1) % 8, 4 + mb % 4)
    fa = 4 * block + i
    w0t = np.ascontiguousarray(np.asarray(L0_rec_W0).T)
    w0t = np.concatenate([w0t, np.zeros((1, 128), w0t.dtype)], axis=0)
    fq = 4 * mb[:, None] + np.arange(4)[None, :]
    w0 = w0t[fa[:, None] * 32 + fq]
    w0swap = w0t[np.where((block != mb)[:, None], fq * 32 + fa[:, None], 1024)]
    wuv = np.concatenate([w0t[f * 32 + 4 * (f // 4) + e] for e in range(4)], axis=0)
    wuv = np.concatenate([wuv, wuv], axis=0)
    w1 = np.asarray(L0_rec_W1).reshape(128, 16, 4, 8, 4).transpose(1, 3, 4, 2, 0).reshape(128, 16, 128)
    sel = np.zeros((128, 4, 128), np.float32)
    r = np.arange(128)
    for ii in range(4):
        sel[4 * (r // 8) + ii, ii, r] = 1
        sel[64 + 4 * (r // 8) + ii, ii, r] = 1

    arrays = {"xT": xT, "w0": w0, "w0swap": w0swap, "w1": w1, "wuv": wuv, "sel": sel,
              "b0": np.asarray(L0_rec_b0).reshape(128, 1), "b1": np.asarray(L0_rec_b1).reshape(128, 1)}
    arrays = {n: np.ascontiguousarray(v) for n, v in arrays.items()}
    nc = bacc.Bacc("TRN2", target_bir_lowering=False, num_devices=1)
    args = [nc.dram_tensor(n, v.shape, mybir.dt.from_np(v.dtype), kind="ExternalInput").ap() for n, v in arrays.items()]
    outT = nc.dram_tensor("outT", (192, B), F32, kind="ExternalOutput").ap()
    build(nc, *args, outT)
    res = run_bass_kernel_spmd(nc, [arrays], core_ids=[0])
    return np.ascontiguousarray(res.results[0]["outT"].T)
```

```python
from contextlib import ExitStack

import concourse.bass as bass
from concourse import mybir

F32 = mybir.dt.float32
F32R = mybir.dt.float32r
ALU = mybir.AluOpType
ACT = mybir.ActivationFunctionType
AX_X = mybir.AxisListType.X

P = 128
N = 512
DIM = 64
BPC = N // DIM
BODY = 4
RING = 4
GPC = 5
LOADS = 5

BY_POOL = (4, 4, 0, 4, 0)
BY_DVE = (0, 0, 0, 0, 2)
SPLIT = tuple(p + d for p, d in zip(BY_POOL, BY_DVE))
NATIVE1 = 8


def past(count, n):
    return not isinstance(count, int) or count >= n


def build(nc, xT, w0, w0swap, w1, wuv, sel, b0, b1, outT):
    S = xT.shape[1]
    CHUNKS = S // N
    BATCH = S // DIM
    assert CHUNKS % BODY == 0 and (BODY * GPC) % RING == 0

    with ExitStack() as ctx:
        def sb(name, shape, dt=F32):
            return ctx.enter_context(nc.sbuf_tensor(name, shape, dt))

        def sem(name):
            return ctx.enter_context(nc.semaphore(name))

        q = sb("q", [P, BODY, 4, N])
        a = sb("a", [P, 2, N])
        uv = sb("uv", [P, 2, 2, N])
        z = sb("z", [P, RING, 4, N])
        zh = sb("zh", [P, RING, 4, N], F32R)
        zl = sb("zl", [P, RING, 4, N], F32R)
        zuv = sb("zuv", [P, 2, N])
        zuvs = sb("zuvs", [P, 2, N], F32R)
        stage = z[:].rearrange("p r s n -> p r (s n)")
        w0_st = stage[:, 0, 0:4 * P].rearrange("p (s n) -> p s n", n=P)
        w0s_st = stage[:, 0, 4 * P:8 * P].rearrange("p (s n) -> p s n", n=P)
        wuv_st = stage[:, 0, 8 * P:9 * P]
        sel_st = stage[:, 1, 0:4 * P].rearrange("p (s n) -> p s n", n=P)
        w1_st = stage[:, 2, :].rearrange("p (s n) -> p s n", n=P)
        w0_sb = sb("w0_sb", [P, 4, P])
        w0h = sb("w0h", [P, 4, P], F32R)
        w0l = sb("w0l", [P, 4, P], F32R)
        w1_sb = sb("w1_sb", [P, 4, P])
        w1h = sb("w1h", [P, 16, P], F32R)
        w1l = sb("w1l", [P, 16, P], F32R)
        wuvh = sb("wuvh", [P, P], F32R)
        wuvl = sb("wuvl", [P, P], F32R)
        selr = sb("selr", [P, 4, P], F32R)
        b0_sb = sb("b0_sb", [P, 1])
        b1_sb = sb("b1_sb", [P, 1])
        r0 = sb("r0", [P, 2, N])
        hs = sb("hs", [P, 2, N], F32R)
        r1 = sb("r1", [P, 2, N])
        sum0 = sb("sum0", [P, BATCH])
        sum1 = sb("sum1", [P, BATCH])

        p_ps = ctx.enter_context(nc.psum_tensor("p_ps", [P, 4, N], F32))
        out0 = ctx.enter_context(nc.psum_tensor("out0", [P, 2, N], F32))
        out1 = ctx.enter_context(nc.psum_tensor("out1", [P, 2, N], F32))

        weights_loaded = sem("weights_loaded")
        x_loaded = [sem(f"x_loaded{s}") for s in range(BODY)]
        wsym_ready = sem("wsym_ready")
        wh_ready = sem("wh_ready")
        wl_ready = sem("wl_ready")
        z_ready = sem("z_ready")
        zh_ready = sem("zh_ready")
        zl_ready = sem("zl_ready")
        zl_pool_ready = sem("zl_pool_ready")
        zuv_ready = sem("zuv_ready")
        zuvh_ready = sem("zuvh_ready")
        zuvl_ready = sem("zuvl_ready")
        group_done = sem("group_done")
        layer0_done = sem("layer0_done")
        r0_ready = sem("r0_ready")
        hh_ready = sem("hh_ready")
        hl_ready = sem("hl_ready")
        p_ready = sem("p_ready")
        r1_ready = sem("r1_ready")
        sum0_ready = sem("sum0_ready")
        sum1_ready = sem("sum1_ready")
        stored = sem("stored")

        block = ctx.enter_context(nc.Block())

        def x_rows(pattern, row, c):
            return bass.AP(xT.tensor, row * S + c * N, [[st * S, n] for st, n in pattern] + [[1, N]])

        def run(eng, chunk):
            for c in range(BODY):
                chunk(c, c)
            with eng.Fori(BODY, CHUNKS - BODY, BODY) as base:
                for k in range(BODY):
                    chunk(base + k, k)
            for k in range(BODY):
                chunk(CHUNKS - BODY + k, k)

        def group1(c, j):
            return c * GPC + 2 + j - (isinstance(c, int) and c == CHUNKS - 1)

        def slot1(c, k, j):
            return (k * GPC + 2 + j - (isinstance(c, int) and c == CHUNKS - 1)) % RING

        def upto(c, j, made):
            each = [n > 0 for n in made]
            return 2 * each[4] + c * sum(each) + sum(each[:j + 1]) - (each[4] and isinstance(c, int) and c == CHUNKS - 1)

        def upto0(c, made):
            if isinstance(c, int) and c < 2:
                return (c + 1) * (made[4] > 0)
            return upto(c - 2, 4, made)

        def visit(c):
            return c // BODY + 1

        @block.sync
        def _(sp):
            def load(c, k):
                if past(c, BODY):
                    sp.wait_ge(z_ready, (c - BODY) * GPC + 6)
                sp.dma_start(q[:, k], x_rows([(0, 16), (4, 8), (1, 4)], 0, c)).then_inc(x_loaded[k], 16)
                if past(c, 2):
                    sp.wait_ge(zuv_ready, c - 1)
                sp.dma_start(a[0:96, k % 2], x_rows([(4, 3), (1, 4), (4, 8)], 4, c)).then_inc(x_loaded[k], 16)
                sp.dma_start(a[96:128, k % 2], x_rows([(1, 4), (4, 8)], 44, c)).then_inc(x_loaded[k], 16)
                sp.dma_start(uv[:, k % 2, 0], x_rows([(0, 8), (1, 16)], 0, c)).then_inc(x_loaded[k], 16)
                sp.dma_start(uv[:, k % 2, 1], x_rows([(0, 2), (1, 64)], 76, c)).then_inc(x_loaded[k], 16)

            run(sp, load)
            sp.wait_ge(sum0_ready, CHUNKS)
            sp.wait_ge(sum1_ready, CHUNKS)
            sp.dma_start(outT[0:64, :], sum0[64:128, :]).then_inc(stored, 16)
            sp.dma_start(outT[64:192, :], sum1[:, :]).then_inc(stored, 16)
            sp.wait_ge(stored, 32)

        @block.scalar
        def _(act):
            for dst, src in ((w0_st, w0), (w0s_st, w0swap), (w1_st, w1), (wuv_st, wuv), (sel_st, sel), (b0_sb[:], b0), (b1_sb[:], b1),
                             (w1_sb[:], w1[:, NATIVE1:NATIVE1 + 4])):
                act.dma_start(dst, src).then_inc(weights_loaded, 16)
            act.wait_ge(weights_loaded, 8 * 16)
            nc.scalar.activation(w1h[:], w1_st, ACT.Copy).then_inc(wh_ready, 1)
            nc.scalar.activation(wuvh[:], wuv_st, ACT.Copy).then_inc(wh_ready, 1)
            nc.scalar.activation(selr[:], sel_st, ACT.Copy).then_inc(wh_ready, 1)
            act.wait_ge(wsym_ready, 1)
            nc.scalar.activation(w0h[:], w0_sb[:], ACT.Copy).then_inc(wh_ready, 1)

            def high(g, j, slot):
                if SPLIT[j]:
                    act.wait_ge(z_ready, g + 1)
                    nc.scalar.activation(zh[:, slot, 0:SPLIT[j]], z[:, slot, 0:SPLIT[j]], ACT.Copy).then_inc(zh_ready, 1)

            def high_uv(c, k):
                act.wait_ge(zuv_ready, c + 1)
                if past(c, 2):
                    act.wait_ge(layer0_done, c - 1)
                nc.scalar.activation(zuvs[:, k % 2], zuv[:, k % 2], ACT.Copy).then_inc(zuvh_ready, 1)

            def relu0(c, k):
                act.wait_ge(layer0_done, c + 1)
                if past(c, 2):
                    act.wait_ge(sum0_ready, c - 1)
                    act.wait_ge(hl_ready, c - 1)
                    act.wait_ge(p_ready, c - 1)
                nc.scalar.activation(r0[:, k % 2], out0[:, k % 2], ACT.Relu, bias=b0_sb[:]).then_inc(r0_ready, 1)
                nc.scalar.activation(hs[0:64, k % 2], out0[0:64, k % 2], ACT.Relu, bias=b0_sb[0:64]).then_inc(hh_ready, 1)

            def relu1(c, k):
                act.wait_ge(group_done, group1(c, 3) + 1)
                if past(c, 2):
                    act.wait_ge(sum1_ready, c - 1)
                nc.scalar.activation(r1[:, k % 2], out1[:, k % 2], ACT.Relu, bias=b1_sb[:]).then_inc(r1_ready, 1)

            high(0, 4, 0)
            high_uv(0, 0)
            high(1, 4, 1)
            high_uv(1, 1)
            relu0(0, 0)

            def chunk(c, k):
                for j in range(4):
                    high(group1(c, j), j, slot1(c, k, j))
                    if j == 0 and past(c, 1):
                        relu1(c - 1, (k - 1) % BODY)
                    if j == 1 and not (isinstance(c, int) and c + 1 >= CHUNKS):
                        relu0(c + 1, (k + 1) % BODY)
                if not (isinstance(c, int) and c + 2 >= CHUNKS):
                    high(c * GPC + 6, 4, (k * GPC + 6) % RING)
                    high_uv(c + 2, k % BODY)

            run(act, chunk)
            relu1(CHUNKS - 1, BODY - 1)

        @block.gpsimd
        def _(pool):
            def low(count, j, slot):
                if BY_POOL[j]:
                    pool.wait_ge(zh_ready, count)
                    nc.gpsimd.tensor_tensor(zl[:, slot, 0:BY_POOL[j]], z[:, slot, 0:BY_POOL[j]],
                                            zh[:, slot, 0:BY_POOL[j]].bitcast(F32), ALU.subtract).then_inc(zl_pool_ready, 1)

            low(1, 4, 0)
            low(2, 4, 1)

            def chunk(c, k):
                for j in range(4):
                    low(upto(c, j, SPLIT), j, slot1(c, k, j))
                if not (isinstance(c, int) and c + 2 >= CHUNKS):
                    low(upto(c, 4, SPLIT), 4, (k * GPC + 6) % RING)

            run(pool, chunk)

        @block.vector
        def _(dve):
            dve.wait_ge(weights_loaded, 8 * 16)
            nc.vector.tensor_tensor(w0_sb[:], w0_st, w0s_st, ALU.add).then_inc(wsym_ready, 1)
            dve.wait_ge(wh_ready, 3)
            nc.vector.tensor_tensor(w1l[:], w1_st, w1h[:].bitcast(F32), ALU.subtract).then_inc(wl_ready, 1)
            nc.vector.tensor_tensor(wuvl[:], wuv_st, wuvh[:].bitcast(F32), ALU.subtract).then_inc(wl_ready, 1)
            dve.wait_ge(wsym_ready, 1)
            dve.wait_ge(wh_ready, 4)
            nc.vector.tensor_tensor(w0l[:], w0_sb[:], w0h[:].bitcast(F32), ALU.subtract).then_inc(wl_ready, 1)
            dve.wait_ge(wl_ready, 3)

            def low(count, j, slot):
                if BY_DVE[j]:
                    dve.wait_ge(zh_ready, count)
                    some = slice(BY_POOL[j], SPLIT[j])
                    nc.vector.tensor_tensor(zl[:, slot, some], z[:, slot, some], zh[:, slot, some].bitcast(F32), ALU.subtract).then_inc(zl_ready, 1)

            def low_uv(c, k):
                dve.wait_ge(zuvh_ready, c + 1)
                nc.vector.tensor_tensor(zuvs[64:128, k % 2], zuv[64:128, k % 2], zuvs[64:128, k % 2].bitcast(F32), ALU.subtract).then_inc(zuvl_ready, 1)

            def products0(c, k, g, slot):
                dve.wait_ge(x_loaded[k], 16 * LOADS * visit(c))
                if past(g, RING):
                    dve.wait_ge(group_done, g - RING + 1)
                nc.vector.tensor_tensor(z[:, slot], a[:, k % 2].unsqueeze(1).to_broadcast([P, 4, N]), q[:, k], ALU.mult).then_inc(z_ready, 1)
                if past(c, 2):
                    dve.wait_ge(layer0_done, c - 1)
                nc.vector.tensor_tensor(zuv[:, k % 2], uv[:, k % 2, 0], uv[:, k % 2, 1], ALU.mult).then_inc(zuv_ready, 1)

            def products1(c, k, j, g, slot):
                if j == 0:
                    dve.wait_ge(p_ready, c + 1)
                if past(g, RING):
                    dve.wait_ge(group_done, g - RING + 1)
                nc.vector.tensor_tensor(z[:, slot], p_ps[:], q[:, k, j].unsqueeze(1).to_broadcast([P, 4, N]), ALU.mult).then_inc(z_ready, 1)

            def low_h(c, k):
                dve.wait_ge(r0_ready, c + 1)
                dve.wait_ge(hh_ready, c + 1)
                nc.vector.tensor_tensor(hs[64:128, k % 2], r0[0:64, k % 2], hs[0:64, k % 2].bitcast(F32), ALU.subtract).then_inc(hl_ready, 1)

            def sums0(c, k):
                nc.vector.tensor_reduce(sum0[64:128, bass.ds(c * BPC, BPC)], r0[64:128, k % 2].rearrange("p (b d) -> p b d", d=DIM), AX_X, ALU.add).then_inc(sum0_ready, 1)

            def sums1(c, k):
                dve.wait_ge(r1_ready, c + 1)
                nc.vector.tensor_reduce(sum1[:, bass.ds(c * BPC, BPC)], r1[:, k % 2].rearrange("p (b d) -> p b d", d=DIM), AX_X, ALU.add).then_inc(sum1_ready, 1)

            products0(0, 0, 0, 0)
            low(1, 4, 0)
            low_uv(0, 0)
            products0(1, 1, 1, 1)
            low_h(0, 0)
            sums0(0, 0)

            def chunk(c, k):
                for j in range(4):
                    products1(c, k, j, group1(c, j), slot1(c, k, j))
                    if j == 0:
                        if not (isinstance(c, int) and c + 1 >= CHUNKS):
                            low(upto0(c + 1, SPLIT), 4, (k * GPC + 1) % RING)
                            low_uv(c + 1, (k + 1) % BODY)
                    else:
                        low(upto(c, j - 1, SPLIT), j - 1, slot1(c, k, j - 1))
                    if j == 2 and not (isinstance(c, int) and c + 1 >= CHUNKS):
                        low_h(c + 1, (k + 1) % BODY)
                if not (isinstance(c, int) and c + 1 >= CHUNKS):
                    sums0(c + 1, (k + 1) % BODY)
                if past(c, 1):
                    sums1(c - 1, (k - 1) % BODY)
                if not (isinstance(c, int) and c + 2 >= CHUNKS):
                    products0(c + 2, (k + 2) % BODY, c * GPC + 6, (k * GPC + 6) % RING)
                low(upto(c, 3, SPLIT), 3, slot1(c, k, 3))

            run(dve, chunk)
            sums1(CHUNKS - 1, BODY - 1)

        @block.tensor
        def _(pe):
            pe.wait_ge(wh_ready, 4)
            pe.wait_ge(wl_ready, 3)

            def contract(out, slot, j, count, starts, stops, w, wh, wl):
                if SPLIT[j]:
                    pe.wait_ge(zh_ready, count(SPLIT))
                for n in range(SPLIT[j]):
                    nc.tensor.matmul(out, wh(n), zh[:, slot, n], start=starts and n == 0, stop=False)
                    last = nc.tensor.matmul(out, wl(n), zh[:, slot, n], start=False, stop=False)
                for n in range(SPLIT[j], 4):
                    last = nc.tensor.matmul(out, w(n), z[:, slot, n], start=starts and n == 0, stop=stops and n == 3 and not SPLIT[j])
                if BY_DVE[j]:
                    pe.wait_ge(zl_ready, count(BY_DVE))
                if BY_POOL[j]:
                    pe.wait_ge(zl_pool_ready, count(BY_POOL))
                for n in range(SPLIT[j]):
                    last = nc.tensor.matmul(out, wh(n), zl[:, slot, n], start=False, stop=stops and n == SPLIT[j] - 1)
                last.then_inc(group_done, 1)

            def contract0(c, k, g, slot):
                if past(c, 2):
                    pe.wait_ge(r0_ready, c - 1)
                    pe.wait_ge(hh_ready, c - 1)
                pe.wait_ge(z_ready, g + 1)
                contract(out0[:, k % 2], slot, 4, lambda made: upto0(c, made), True, False,
                         lambda n: w0_sb[:, n], lambda n: w0h[:, n], lambda n: w0l[:, n])
                pe.wait_ge(zuvh_ready, c + 1)
                pe.wait_ge(zuvl_ready, c + 1)
                nc.tensor.matmul(out0[:, k % 2], wuvh[:], zuvs[:, k % 2], start=False, stop=False)
                nc.tensor.matmul(out0[:, k % 2], wuvl[:], zuvs[:, k % 2], start=False, stop=True).then_inc(layer0_done, 1)

            def contract1(c, k, j, g, slot):
                if j == 0 and past(c, 2):
                    pe.wait_ge(r1_ready, c - 1)
                pe.wait_ge(z_ready, g + 1)
                contract(out1[:, k % 2], slot, j, lambda made: upto(c, j, made), j == 0, j == 3,
                         lambda n: w1_sb[:, 4 * j + n - NATIVE1], lambda n: w1h[:, 4 * j + n], lambda n: w1l[:, 4 * j + n])

            def select(c, k):
                pe.wait_ge(hl_ready, c + 1)
                pe.wait_ge(hh_ready, c + 1)
                if past(c, 1):
                    pe.wait_ge(z_ready, c * GPC + 1)
                for i in range(4):
                    last = nc.tensor.matmul(p_ps[:, i], selr[:, i], hs[:, k % 2], start=True, stop=True)
                last.then_inc(p_ready, 1)

            contract0(0, 0, 0, 0)
            select(0, 0)
            contract0(1, 1, 1, 1)

            def chunk(c, k):
                for j in range(4):
                    contract1(c, k, j, group1(c, j), slot1(c, k, j))
                    if j == 1 and not (isinstance(c, int) and c + 1 >= CHUNKS):
                        select(c + 1, (k + 1) % BODY)
                if not (isinstance(c, int) and c + 2 >= CHUNKS):
                    contract0(c + 2, (k + 2) % BODY, c * GPC + 6, (k * GPC + 6) % RING)

            run(pe, chunk)


def kernel(r_inputs, L0_rec_W0, L0_rec_b0, L0_rec_W1, L0_rec_b1):
    import numpy as np
    import concourse.bacc as bacc
    from concourse.bass_utils import run_bass_kernel_spmd

    x = np.asarray(r_inputs)
    B, M, D = x.shape
    xT = np.ascontiguousarray(np.transpose(x, (1, 0, 2))).reshape(M, B * D)
    f = np.arange(16)
    xT = np.concatenate([xT, xT[0:12], xT[16:32], xT[16:32]] + [xT[4 * (f // 4) + e] for e in range(4)], axis=0)

    s, i, mb = (t.reshape(-1) for t in np.meshgrid(np.arange(4), np.arange(4), np.arange(8), indexing="ij"))
    block = np.where(s < 3, (mb + s + 1) % 8, 4 + mb % 4)
    fa = 4 * block + i
    w0t = np.ascontiguousarray(np.asarray(L0_rec_W0).T)
    w0t = np.concatenate([w0t, np.zeros((1, 128), w0t.dtype)], axis=0)
    fq = 4 * mb[:, None] + np.arange(4)[None, :]
    w0 = w0t[fa[:, None] * 32 + fq]
    w0swap = w0t[np.where((block != mb)[:, None], fq * 32 + fa[:, None], 1024)]
    wuv = np.concatenate([w0t[f * 32 + 4 * (f // 4) + e] for e in range(4)], axis=0)
    wuv = np.concatenate([wuv, wuv], axis=0)
    w1 = np.asarray(L0_rec_W1).reshape(128, 16, 4, 8, 4).transpose(1, 3, 4, 2, 0).reshape(128, 16, 128)
    sel = np.zeros((128, 4, 128), np.float32)
    r = np.arange(128)
    for ii in range(4):
        sel[4 * (r // 8) + ii, ii, r] = 1
        sel[64 + 4 * (r // 8) + ii, ii, r] = 1

    arrays = {"xT": xT, "w0": w0, "w0swap": w0swap, "w1": w1, "wuv": wuv, "sel": sel,
              "b0": np.asarray(L0_rec_b0).reshape(128, 1), "b1": np.asarray(L0_rec_b1).reshape(128, 1)}
    arrays = {n: np.ascontiguousarray(v) for n, v in arrays.items()}
    nc = bacc.Bacc("TRN2", target_bir_lowering=False, num_devices=1)
    args = [nc.dram_tensor(n, v.shape, mybir.dt.from_np(v.dtype), kind="ExternalInput").ap() for n, v in arrays.items()]
    outT = nc.dram_tensor("outT", (192, B), F32, kind="ExternalOutput").ap()
    build(nc, *args, outT)
    res = run_bass_kernel_spmd(nc, [arrays], core_ids=[0])
    return np.ascontiguousarray(res.results[0]["outT"].T)
```

```python
from contextlib import ExitStack

import concourse.bass as bass
from concourse import mybir

F32 = mybir.dt.float32
F32R = mybir.dt.float32r
ALU = mybir.AluOpType
ACT = mybir.ActivationFunctionType
AX_X = mybir.AxisListType.X

P = 128
N = 512
H = 64
DIM = 64
BPC = N // DIM
BODY = 4
LEAD = 3
RING = 4
GPC = 5
SPLIT1 = 3
SPLIT0 = (2, 1, 2, 1)
assert LEAD < BODY == len(SPLIT0) and (BODY * GPC) % RING == 0

PAIRS = 40
COPY1, COPY2, COPY3 = [(0, 0, 40)], [(40, 0, 24), (104, 24, 16)], [(64, 0, 40)]


def past(count, n):
    return not isinstance(count, int) or count >= n


def build(nc, fields, spread, w0, w0swap, w1, takes, b0, b1, outT):
    S = fields.shape[1]
    CHUNKS = S // N
    BATCH = S // DIM
    assert CHUNKS % BODY == 0

    with ExitStack() as ctx:
        def sb(name, shape, dt=F32):
            return ctx.enter_context(nc.sbuf_tensor(name, shape, dt))

        def ps(name, shape):
            return ctx.enter_context(nc.psum_tensor(name, shape, F32))

        def sem(name):
            return ctx.enter_context(nc.semaphore(name))

        qv = sb("qv", [P, BODY, 5, N])
        au = sb("au", [P, 2, 2, N])
        z = sb("z", [P, RING, 4, N])
        zh = sb("zh", [P, RING, SPLIT1, N], F32R)
        zl = sb("zl", [P, RING, SPLIT1, N], F32R)
        pair_h = sb("pair_h", [P, 2, N], F32R)
        pair_l = sb("pair_l", [P, N], F32R)
        h = sb("h", [H, 2, N])
        p_sb = sb("p_sb", [P, 2, 4, N])
        r1 = sb("r1", [P, N])
        staged_w1 = p_sb[:, 1].rearrange("p i n -> p (i n)").rearrange("p (s o) -> p s o", o=P)
        staged = z[:, RING - 1].rearrange("p s n -> p (s n)").rearrange("p (s o) -> p s o", o=P)
        staged_w0, staged_w0swap = staged[:, 0:5], staged[:, 5:10]
        w0f = sb("w0f", [P, 5, P])
        w0h = sb("w0h", [P, 5, P], F32R)
        w0l = sb("w0l", [P, 5, P], F32R)
        wuv_low = sb("wuv_low", [P, P])
        wuv = sb("wuv", [P, P], F32R)
        w1f = sb("w1f", [P, 4, P])
        w1h = sb("w1h", [P, 16, P], F32R)
        w1l = sb("w1l", [P, 16, P], F32R)
        takes_sb = sb("takes_sb", [P, 2])
        b0_sb = sb("b0_sb", [P, 1])
        b1_sb = sb("b1_sb", [P, 1])
        sum0 = sb("sum0", [P, BATCH + BODY * BPC])
        sum1 = sb("sum1", [P, BATCH])

        p_ps = ps("p_ps", [P, 4, N])
        au_ps = ps("au_ps", [P, 2, N])
        out0 = ps("out0", [P, N])
        out1 = ps("out1", [P, N])

        w0_loaded = sem("w0_loaded")
        w1_loaded = sem("w1_loaded")
        qv_loaded = [sem(f"qv_loaded{s}") for s in range(BODY)]
        au_loaded = [sem(f"au_loaded{s}") for s in range(BODY)]
        w0f_ready = sem("w0f_ready")
        w0h_ready = sem("w0h_ready")
        w0l_ready = sem("w0l_ready")
        w1h_ready = sem("w1h_ready")
        w1l_ready = sem("w1l_ready")
        au_ready = sem("au_ready")
        z_ready = sem("z_ready")
        zh_ready = sem("zh_ready")
        zl1_ready = sem("zl1_ready")
        zl0_pool_ready = sem("zl0_pool_ready")
        zl0_ready = sem("zl0_ready")
        pair_ready = sem("pair_ready")
        pair_h_ready = sem("pair_h_ready")
        pair_l_ready = sem("pair_l_ready")
        group_done = sem("group_done")
        layer0_done = sem("layer0_done")
        h_ready = sem("h_ready")
        p_spread = [sem(f"p_spread{s}") for s in range(2)]
        p_ready = sem("p_ready")
        r1_ready = sem("r1_ready")
        sum0_ready = sem("sum0_ready")
        sum1_ready = sem("sum1_ready")
        stored = sem("stored")

        block = ctx.enter_context(nc.Block())


        def is_last(c, n=1):
            return isinstance(c, int) and c >= CHUNKS - n

        def leads(c):
            return LEAD + (min(c, CHUNKS - LEAD) if isinstance(c, int) else c)

        def group1(c, j):
            return 4 * c + leads(c) + j

        def slot1(c, k, j):
            return (group1(c, j) if isinstance(c, int) else k * GPC + LEAD + j) % RING

        def group0(c):
            return c if isinstance(c, int) and c < LEAD else c * GPC + 4 - 4 * LEAD

        def slot0(c, k):
            return (group0(c) if isinstance(c, int) else k * GPC + 4 - 4 * LEAD) % RING

        def run(eng, chunk):
            for k in range(BODY):
                chunk(k, k)
            with eng.Fori(BODY, CHUNKS - BODY, BODY) as base:
                for k in range(BODY):
                    chunk(base + k, k)
            for k in range(BODY):
                chunk(CHUNKS - BODY + k, k)

        def next_(k, n=1):
            return (k + n) % BODY

        @block.sync
        def _(sp):
            def load_au(c, k):
                if past(c, 2):
                    sp.wait_ge(au_ready, c - 1)
                sp.dma_start(au[:, k % 2], spread[0:2, :, bass.ds(c * N, N)].rearrange("a p n -> p a n")).then_inc(au_loaded[k], 16)

            def load_qv(c, k):
                if past(c, BODY):
                    sp.wait_ge(z_ready, (c - BODY) * GPC + LEAD + 4)
                sp.dma_start(qv[:, k, 0:4], bass.AP(fields.tensor, c * N, [[0, 16], [4 * S, 8], [S, 4], [1, N]])).then_inc(qv_loaded[k], 16)
                sp.dma_start(qv[:, k, 4], spread[2, :, bass.ds(c * N, N)]).then_inc(qv_loaded[k], 16)

            def spread_h(c, k):
                sp.wait_ge(h_ready, c + 1)
                for i in range(4):
                    sp.dma_start(p_sb[:, k % 2, i], h[i:H:4, k % 2].unsqueeze(1).to_broadcast([H // 4, 8, N])).then_inc(p_spread[k % 2], 16)

            def chunk(c, k):
                if not past(c, LEAD):
                    load_qv(c, k)
                if not is_last(c):
                    load_au(c + 1, next_(k))
                if isinstance(c, int) and c == 3:
                    sp.wait_ge(w1l_ready, 1)
                if past(c, 2):
                    spread_h(c - 2, next_(k, -2))
                if past(c, LEAD):
                    load_qv(c, k)

            sp.dma_start(staged_w0, w0).then_inc(w0_loaded, 16)
            sp.dma_start(staged_w0swap, w0swap).then_inc(w0_loaded, 16)
            load_au(0, 0)
            run(sp, chunk)
            spread_h(CHUNKS - 2, BODY - 2)
            spread_h(CHUNKS - 1, BODY - 1)
            sp.wait_ge(sum0_ready, CHUNKS)
            sp.wait_ge(sum1_ready, CHUNKS)
            sp.dma_start(outT[0:64, :], sum0[H:P, 0:BATCH]).then_inc(stored, 16)
            sp.dma_start(outT[64:192, :], sum1[:, :]).then_inc(stored, 16)
            sp.wait_ge(stored, 32)

        @block.scalar
        def _(act):
            act.dma_start(takes_sb[:], takes).then_inc(w0_loaded, 16)
            act.dma_start(b0_sb[:], b0).then_inc(w0_loaded, 16)

            def fetch(c, k):
                act.wait_ge(au_loaded[k], 16 * (c // BODY + 1))
                if past(c, 1):
                    act.wait_ge(pair_l_ready, 2 * c)
                nc.scalar.activation(au_ps[:], au[:, k % 2], ACT.Copy).then_inc(au_ready, 1)

            def high(group, slot, split):
                act.wait_ge(z_ready, group + 1)
                nc.scalar.activation(zh[:, slot, 0:split], z[:, slot, 0:split], ACT.Copy).then_inc(zh_ready, 1)

            def high1(c, k, i):
                high(group1(c, i), slot1(c, k, i), SPLIT1)

            def high0(c, k):
                high(group0(c), slot0(c, k), SPLIT0[k])

            def high_pair(c):
                act.wait_ge(pair_ready, c + 1)
                if past(c, 1):
                    act.wait_ge(layer0_done, c)
                nc.scalar.activation(pair_h[:], au_ps[:], ACT.Copy).then_inc(pair_h_ready, 1)

            def relu_h(c, k):
                act.wait_ge(layer0_done, c + 1)
                nc.scalar.activation(h[:, k % 2], out0[0:H], ACT.Relu, bias=b0_sb[0:H]).then_inc(h_ready, 1)

            def fetch_p(c, k, half):
                if half == 0:
                    act.wait_ge(p_spread[k % 2], 4 * 16 * (c // 2 + 1))
                if past(c, 1):
                    act.wait_ge(z_ready, group1(c - 1, 2 * half + 1) + 1)
                some = slice(2 * half, 2 * half + 2)
                nc.scalar.activation(p_ps[:, some], p_sb[:, k % 2, some], ACT.Copy).then_inc(p_ready, 1)

            def sums0(c):
                for b in range(BPC):
                    row = out0[H:P, b * DIM:(b + 1) * DIM]
                    last = nc.scalar.activation(row, row, ACT.Relu, bias=b0_sb[H:P],
                                                accum_out=sum0[H:P, bass.ds(c * BPC + b, 1)])
                last.then_inc(sum0_ready, 1)

            def relu1(c):
                act.wait_ge(group_done, group1(c, 3) + 1)
                if past(c, 1):
                    act.wait_ge(sum1_ready, c)
                nc.scalar.activation(r1[:], out1[:], ACT.Relu, bias=b1_sb[:]).then_inc(r1_ready, 1)

            fetch(0, 0)
            act.wait_ge(w0f_ready, 1)
            nc.scalar.activation(w0h[:], w0f[:], ACT.Copy).then_inc(w0h_ready, 1)
            high0(0, 0)
            high_pair(0)
            fetch(1, 1)
            high0(1, 1)
            relu_h(0, 0)
            high_pair(1)
            sums0(0)
            fetch(2, 2)
            high0(2, 2)
            act.wait_ge(w1_loaded, 3 * 16)
            nc.scalar.activation(w1h[:], staged_w1, ACT.Copy).then_inc(w1h_ready, 1)
            relu_h(1, 1)
            sums0(1)
            high_pair(2)
            fetch_p(0, 0, 0)
            fetch_p(0, 0, 1)

            def chunk(c, k):
                high1(c, k, 0)
                if not is_last(c, LEAD):
                    fetch(c + LEAD, next_(k, LEAD))
                if past(c, 1):
                    relu1(c - 1)
                high1(c, k, 1)
                if not is_last(c):
                    fetch_p(c + 1, next_(k), 0)
                if not is_last(c, 2):
                    relu_h(c + 2, next_(k, 2))
                high1(c, k, 2)
                high1(c, k, 3)
                if not is_last(c, 2):
                    sums0(c + 2)
                if not is_last(c, LEAD):
                    high0(c + LEAD, next_(k, LEAD))
                    high_pair(c + LEAD)
                if not is_last(c):
                    fetch_p(c + 1, next_(k), 1)

            run(act, chunk)
            relu1(CHUNKS - 1)

        @block.gpsimd
        def _(pool):
            pool.wait_ge(qv_loaded[0], 2 * 16)
            for dst, src in ((staged_w1, w1), (b1_sb[:], b1), (w1f[:], w1.rearrange("p (i j) o -> p i j o", i=4)[:, :, 3])):
                pool.dma_start(dst, src).then_inc(w1_loaded, 16)

            def low0(c, k):
                if SPLIT0[k] > 1:
                    slot = slot0(c, k)
                    pool.wait_ge(zh_ready, group0(c) + 1)
                    nc.gpsimd.tensor_tensor(zl[:, slot, 1], z[:, slot, 1], zh[:, slot, 1].bitcast(F32), ALU.subtract).then_inc(zl0_pool_ready, 1)

            def low1(c, k, i):
                slot = slot1(c, k, i)
                pool.wait_ge(zh_ready, group1(c, i) + 1)
                nc.gpsimd.tensor_tensor(zl[:, slot], z[:, slot, 0:SPLIT1], zh[:, slot].bitcast(F32), ALU.subtract).then_inc(zl1_ready, 1)

            def chunk(c, k):
                for i in range(4):
                    low1(c, k, i)
                if not is_last(c, LEAD):
                    low0(c + LEAD, next_(k, LEAD))

            for c in range(LEAD):
                low0(c, c)
            run(pool, chunk)

        @block.vector
        def _(dve):
            def products0(c, k):
                slot = slot0(c, k)
                dve.wait_ge(qv_loaded[k], 2 * 16 * (c // BODY + 1))
                dve.wait_ge(au_ready, c + 1)
                if past(c, LEAD):
                    dve.wait_ge(group_done, group0(c) - RING + 1)
                nc.vector.tensor_tensor(z[:, slot, 0:3], au_ps[:, 0].unsqueeze(1).to_broadcast([P, 3, N]), qv[:, k, 0:3], ALU.mult).then_inc(z_ready, 1)

            def products_pair(c, k):
                dve.wait_ge(z_ready, group0(c) + 1)
                nc.vector.tensor_tensor(au_ps[:], au_ps[:], qv[:, k, 3:5], ALU.mult).then_inc(pair_ready, 1)

            def products1(c, k, i):
                slot = slot1(c, k, i)
                if i % 2 == 0:
                    dve.wait_ge(p_ready, 2 * c + i // 2 + 1)
                if past(group1(c, i), RING):
                    dve.wait_ge(group_done, group1(c, i) - RING + 1)
                nc.vector.tensor_tensor(z[:, slot], p_ps[:, i].unsqueeze(1).to_broadcast([P, 4, N]), qv[:, k, 0:4], ALU.mult).then_inc(z_ready, 1)

            def low0(c, k):
                slot = slot0(c, k)
                dve.wait_ge(zh_ready, group0(c) + 1)
                nc.vector.tensor_tensor(zl[:, slot, 0], z[:, slot, 0], zh[:, slot, 0].bitcast(F32), ALU.subtract).then_inc(zl0_ready, 1)

            def low_pair(c):
                dve.wait_ge(pair_h_ready, c + 1)
                nc.vector.tensor_tensor(pair_h[64:64 + PAIRS, 1], au_ps[64:64 + PAIRS, 1], pair_h[64:64 + PAIRS, 1].bitcast(F32), ALU.subtract).then_inc(pair_l_ready, 1)
                nc.vector.tensor_tensor(pair_l[:], au_ps[:, 0], pair_h[:, 0].bitcast(F32), ALU.subtract).then_inc(pair_l_ready, 1)

            def sums1(c):
                dve.wait_ge(r1_ready, c + 1)
                nc.vector.tensor_reduce(sum1[:, bass.ds(c * BPC, BPC)], r1[:].rearrange("p (b d) -> p b d", d=DIM), AX_X, ALU.add).then_inc(sum1_ready, 1)

            dve.wait_ge(w0_loaded, 4 * 16)
            nc.vector.tensor_tensor(w0f[:], staged_w0, staged_w0swap, ALU.add).then_inc(w0f_ready, 1)
            dve.wait_ge(w0h_ready, 1)
            nc.vector.tensor_tensor(w0l[:], w0f[:], w0h[:].bitcast(F32), ALU.subtract).then_inc(w0l_ready, 1)
            dve.wait_ge(w0l_ready, 1)
            nc.vector.tensor_scalar(wuv_low[:], w0l[:, 4].bitcast(F32), takes_sb[:, 1:2], None, ALU.mult).then_inc(w0l_ready, 1)
            dve.wait_ge(w0l_ready, 2)
            nc.vector.scalar_tensor_tensor(wuv[:], w0h[:, 4].bitcast(F32), takes_sb[:, 0:1], wuv_low[:], ALU.mult, ALU.add).then_inc(w0l_ready, 1)
            products0(0, 0)
            products_pair(0, 0)
            low0(0, 0)
            low_pair(0)
            products0(1, 1)
            products_pair(1, 1)
            low0(1, 1)
            low_pair(1)
            products0(2, 2)
            products_pair(2, 2)
            dve.wait_ge(w1h_ready, 1)
            nc.vector.tensor_tensor(w1l[:], staged_w1, w1h[:].bitcast(F32), ALU.subtract).then_inc(w1l_ready, 1)
            low0(2, 2)
            low_pair(2)

            def chunk(c, k):
                products1(c, k, 0)
                if past(c, 1) and not is_last(c, 2):
                    low0(c + 2, next_(k, 2))
                    low_pair(c + 2)
                products1(c, k, 1)
                products1(c, k, 2)
                products1(c, k, 3)
                if past(c, 1):
                    sums1(c - 1)
                if not is_last(c, LEAD):
                    products0(c + LEAD, next_(k, LEAD))
                    products_pair(c + LEAD, next_(k, LEAD))

            run(dve, chunk)
            sums1(CHUNKS - 1)

        @block.tensor
        def _(pe):
            def contract1(c, k, i):
                slot = slot1(c, k, i)
                if i == 0 and past(c, 1):
                    pe.wait_ge(r1_ready, c)
                pe.wait_ge(zh_ready, group1(c, i) + 1)
                for j in range(SPLIT1):
                    nc.tensor.matmul(out1[:], w1h[:, 4 * i + j], zh[:, slot, j], start=i == 0 and j == 0, stop=False)
                    nc.tensor.matmul(out1[:], w1l[:, 4 * i + j], zh[:, slot, j], start=False, stop=False)
                nc.tensor.matmul(out1[:], w1f[:, i], z[:, slot, 3], start=False, stop=False)
                pe.wait_ge(zl1_ready, 4 * c + i + 1)
                for j in range(SPLIT1):
                    last = nc.tensor.matmul(out1[:], w1h[:, 4 * i + j], zl[:, slot, j], start=False, stop=i == 3 and j == SPLIT1 - 1)
                last.then_inc(group_done, 1)

            def contract0(c, k):
                slot = slot0(c, k)
                if past(c, 1):
                    pe.wait_ge(h_ready, c)
                    pe.wait_ge(sum0_ready, c)
                pe.wait_ge(zh_ready, group0(c) + 1)
                for j in range(SPLIT0[k]):
                    nc.tensor.matmul(out0[:], w0h[:, j], zh[:, slot, j], start=j == 0, stop=False)
                    nc.tensor.matmul(out0[:], w0l[:, j], zh[:, slot, j], start=False, stop=False)
                for j in range(SPLIT0[k], 3):
                    nc.tensor.matmul(out0[:], w0f[:, j], z[:, slot, j], start=False, stop=False)
                pe.wait_ge(pair_h_ready, c + 1)
                nc.tensor.matmul(out0[:], w0h[:, 3], pair_h[:, 0], start=False, stop=False)
                nc.tensor.matmul(out0[:], w0l[:, 3], pair_h[:, 0], start=False, stop=False)
                pe.wait_ge(zl0_ready, c + 1)
                if SPLIT0[k] > 1:
                    pe.wait_ge(zl0_pool_ready, c // 2 + 1)
                for j in range(SPLIT0[k]):
                    last = nc.tensor.matmul(out0[:], w0h[:, j], zl[:, slot, j], start=False, stop=False)
                last.then_inc(group_done, 1)
                pe.wait_ge(pair_l_ready, 2 * (c + 1))
                nc.tensor.matmul(out0[:], w0h[:, 3], pair_l[:], start=False, stop=False)
                nc.tensor.matmul(out0[:], wuv[:], pair_h[:, 1], start=False, stop=True).then_inc(layer0_done, 1)

            pe.wait_ge(w0h_ready, 1)
            pe.wait_ge(w0l_ready, 3)
            for c in range(LEAD):
                contract0(c, c)
            pe.wait_ge(w1_loaded, 3 * 16)
            pe.wait_ge(w1h_ready, 1)
            pe.wait_ge(w1l_ready, 1)

            def chunk(c, k):
                for i in range(4):
                    contract1(c, k, i)
                if not is_last(c, LEAD):
                    contract0(c + LEAD, next_(k, LEAD))

            run(pe, chunk)


def kernel(r_inputs, L0_rec_W0, L0_rec_b0, L0_rec_W1, L0_rec_b1):
    import numpy as np
    import concourse.bacc as bacc
    from concourse.bass_utils import run_bass_kernel_spmd

    x = np.asarray(r_inputs)
    B, M, D = x.shape
    fields = np.ascontiguousarray(np.transpose(x, (1, 0, 2))).reshape(M, B * D)
    pairs = np.array([(4 * k + i, 4 * k + j) for k in range(4) for i in range(4) for j in range(i, 4)])

    s, i, mb = (t.reshape(-1) for t in np.meshgrid(np.arange(4), np.arange(4), np.arange(8), indexing="ij"))
    block = np.where(s < 3, (mb + s + 1) % 8, 4 + mb % 4)
    fa = (4 * block + i)[:, None]
    fq = 4 * mb[:, None] + np.arange(4)[None, :]
    w0t = np.concatenate([np.asarray(L0_rec_W0).T, np.zeros((1, 128), np.float32)], axis=0)
    uv = np.zeros((P, 2), int)
    rows = np.full((P, 5), 1024)
    swapped = np.full((P, 5), 1024)
    rows[:, 0:4] = fa * 32 + fq
    swapped[:, 0:4] = np.where(block[:, None] != mb[:, None], fq * 32 + fa, 1024)
    takes = np.zeros((P, 2), np.float32)
    for part, copy in ((0, COPY1), (1, COPY2), (0, COPY3)):
        for first, pair, n in copy:
            u, v = pairs[pair:pair + n, 0], pairs[pair:pair + n, 1]
            uv[first:first + n] = pairs[pair:pair + n]
            rows[first:first + n, 4] = u * 32 + v
            swapped[first:first + n, 4] = np.where(u != v, v * 32 + u, 1024)
            takes[first:first + n, part] = 1
    w1 = np.asarray(L0_rec_W1).reshape(128, 16, 4, 8, 4).transpose(1, 3, 2, 4, 0).reshape(128, 16, 128)
    spread = fields[np.stack([fa[:, 0], uv[:, 0], uv[:, 1]])]

    arrays = {"fields": fields, "spread": spread, "w0": w0t[rows], "w0swap": w0t[swapped], "w1": w1, "takes": takes,
              "b0": np.asarray(L0_rec_b0).reshape(128, 1), "b1": np.asarray(L0_rec_b1).reshape(128, 1)}
    arrays = {name: np.ascontiguousarray(a) for name, a in arrays.items()}
    nc = bacc.Bacc("TRN2", target_bir_lowering=False, num_devices=1)
    args = [nc.dram_tensor(name, a.shape, mybir.dt.from_np(a.dtype), kind="ExternalInput").ap() for name, a in arrays.items()]
    outT = nc.dram_tensor("outT", (192, B), F32, kind="ExternalOutput").ap()
    build(nc, *args, outT)
    res = run_bass_kernel_spmd(nc, [arrays], core_ids=[0])
    return np.ascontiguousarray(res.results[0]["outT"].T)
```
